# Optimizing a Trainium2 kernel written in Bass

```python
import numpy as np
import jax
import jax.numpy as jnp

def _softmax(x, axis=-1):
    return jax.nn.softmax(x, axis=axis)

def _gelu(x):
    return jax.nn.gelu(x, approximate=True)

def _silu(x):
    return jax.nn.silu(x)

def _sigmoid(x):
    return jax.nn.sigmoid(x)

def _layernorm(x, axis=-1, eps=1e-05):
    m = jnp.mean(x, axis=axis, keepdims=True)
    v = jnp.var(x, axis=axis, keepdims=True)
    return (x - m) / jnp.sqrt(v + eps)

def _scatter_add(tgt, idx, src, axis=0):
    return tgt.at[idx].add(src)

def _segment_sum(src, seg, n):
    return jax.ops.segment_sum(src, seg, n)
kernel_name = 'mk_adj_preln_d1_adj_r2_062b97'

def setup_inputs(seed: int=0):
    np.random.seed(seed)
    _w = jnp.asarray

    def _rec_inputs():
        import jax
        import jax.numpy as jnp
        _gk = jax.random.key(seed)
        x = -0.001003 + 1 * jax.random.normal(jax.random.fold_in(_gk, 1), (6144, 128), jnp.float32)
        _a = jax.random.bernoulli(jax.random.fold_in(_gk, 2), 0.00260417, (6144, 6144))
        adj = _a.astype(jnp.int32)
        return (x, adj)
    x, adj = _rec_inputs()

    def _L0_gnn_setup():
        import jax, jax.numpy as jnp
        import numpy as np
        M = 6144
        N = 6144
        D = 128
        TEMPERATURE = 0.07
        NEG_PAD = jnp.float32(-2 ** 32 + 1)
        key = jax.random.key(seed)
        k1, k2, k3, k4 = jax.random.split(key, 4)
        xx_anchor = jax.random.normal(k1, (M, D), dtype=jnp.float32)
        inp = jax.random.normal(k2, (N, D), dtype=jnp.float32)
        adj = (jax.random.uniform(k3, (M, N)) < 0.002).astype(jnp.int32)
        limit = jnp.sqrt(6.0 / (D + D)).astype(jnp.float32)
        weight = jax.random.uniform(k4, (D, D), minval=-limit, maxval=limit, dtype=jnp.float32)
        return {'xx_anchor': xx_anchor, 'input': inp, 'adj': adj, 'weight': weight}
    _L0_gnn_all = _L0_gnn_setup()
    _L0_gnn_in = {k: v for k, v in _L0_gnn_all.items() if k in ('input', 'weight')}
    del _L0_gnn_all
    return {'x': x, 'adj': adj, 'L0_gnn_input': _L0_gnn_in['input'], 'L0_gnn_weight': _L0_gnn_in['weight']}

def reference(x, adj, L0_gnn_input, L0_gnn_weight):
    import jax
    import jax.numpy as jnp

    def _L0_gnn_ref(xx_anchor, input, adj, weight):
        import jax, jax.numpy as jnp
        import numpy as np
        M = 6144
        N = 6144
        D = 128
        TEMPERATURE = 0.07
        NEG_PAD = jnp.float32(-2 ** 32 + 1)
        anchor_adj = jnp.einsum('md,de,ne->mn', xx_anchor, weight, input)
        scores = jnp.where(adj > 0, anchor_adj, NEG_PAD)
        atten = jax.nn.softmax(scores / TEMPERATURE, axis=1)
        return atten @ input
    h = jnp.maximum(_layernorm(x, axis=-1), 0.0)
    x = x + _L0_gnn_ref(h, L0_gnn_input, adj, L0_gnn_weight)
    return x

_drawn_inputs = setup_inputs


def setup_inputs(seed=0):
    import zlib

    import numpy as np

    out = dict(_drawn_inputs(seed))
    spreads = {}
    factors = {}
    for name, (base, spread) in spreads.items():
        noise = np.random.default_rng([zlib.crc32(name.encode()), seed]).standard_normal(out[name].shape)
        drawn = base * np.exp(spread * noise) if base else spread * noise
        out[name] = jnp.asarray(drawn.astype(out[name].dtype))
    for name, factor in factors.items():
        out[name] = (out[name] * factor).astype(out[name].dtype)
    return out
```

```python
from contextlib import ExitStack

import concourse.bass as bass
from concourse import mybir

ALU = mybir.AluOpType
ACT = mybir.ActivationFunctionType
AX_X = mybir.AxisListType.X
F32 = mybir.dt.float32
F32R = mybir.dt.float32r
BF16 = mybir.dt.bfloat16
I32 = mybir.dt.int32

P = 128
BANK = 512
UNIT = 2 * BANK
TEMPERATURE = 0.07
EPS = 1e-5
MASKED = -(2.0 ** 100)
LOWEST = -3.0e38

ADJ_RING = 4
MASK_RING = 3
PT_RING = 4


def gnn_attention(nc, x, adj, inp, weight, out):
    M, D = x.shape
    N = inp.shape[0]
    RB = M // P
    CH = N // P
    UNITS = N // UNIT
    STEPS = N // BANK
    CPS = BANK // P
    T_LAG = STEPS + 2
    PV_LAG = T_LAG + 2
    assert D == P and M % (2 * P) == 0 and N % UNIT == 0
    assert STEPS % PT_RING == 0 and UNITS % MASK_RING == 0 and 2 * UNITS % ADJ_RING == 0

    with ExitStack() as ctx:
        def sb(name, shape, dt):
            return ctx.enter_context(nc.sbuf_tensor(name, shape, dt))

        def psum(name, shape, dt):
            return ctx.enter_context(nc.psum_tensor(name, shape, dt))

        def sem(name):
            return ctx.enter_context(nc.semaphore(name))

        v_hilo = sb("v_hilo", [P, CH, 2, D], F32R)
        vt_hi = sb("vt_hi", [P, N], F32R)
        vt_lo = sb("vt_lo", [P, N], F32R)
        probs = sb("probs", [P, 2, N], F32)
        adj_in = sb("adj_in", [P, ADJ_RING, UNIT], I32)
        mask_add = sb("mask_add", [P, MASK_RING, UNIT], BF16)
        pt_hi = sb("pt_hi", [P, PT_RING, BANK], F32R)
        pt_lo = sb("pt_lo", [P, PT_RING, BANK], F32R)
        w_sb = sb("w_sb", [P, D], F32)
        ident = sb("ident", [P, P], F32)
        x_ln = sb("x_ln", [P, 2, D], F32)
        x_res = sb("x_res", [P, 2, D], F32)
        h_norm = sb("h_norm", [P, D], F32)
        h_t = sb("h_t", [P, P], F32)
        q_full = sb("q_full", [P, P], F32)
        q_hi = sb("q_hi", [P, 2, P], F32R)
        q_lo = sb("q_lo", [P, 2, P], F32R)
        stats = sb("stats", [P, RB, 6], F32)
        moments = sb("moments", [P, RB, 2], F32)
        block_moments = sb("block_moments", [P, 2], F32)
        stat_a = sb("stat_a", [P, RB], F32)
        stat_b = sb("stat_b", [P, RB], F32)
        unit_max = sb("unit_max", [P, 2, UNITS], F32)
        neg_max = sb("neg_max", [P, 2], F32)
        unit_sum = sb("unit_sum", [P, 2, UNITS], F32)
        row_sum = sb("row_sum", [P, 2], F32)
        inv_sum = sb("inv_sum", [P, 2], F32)
        out_part = sb("out_part", [P, D], F32)
        out_sb = sb("out_sb", [P, 2, D], F32)

        ps_scores = psum("ps_scores", [P, 2, UNIT], F32)
        ps_pt = psum("ps_pt", [P, 2, BANK], F32)
        ps_out = psum("ps_out", [P, 2, BANK], F32)

        def ps_ht(b_par):
            return ps_out[:, (b_par + 1) % 2, 0:P]

        def ps_q(b_par):
            return ps_out[:, (b_par + 1) % 2, P:2 * P]

        v_loaded = [sem(f"v_loaded{u}") for u in range(UNITS)]
        x_loaded = [sem(f"x_loaded{u}") for u in range(2)]
        w_loaded = sem("w_loaded")
        x_ln_loaded = [sem(f"x_ln_loaded{s}") for s in range(2)]
        x_res_loaded = [sem(f"x_res_loaded{s}") for s in range(2)]
        adj_loaded = [sem(f"adj_loaded{s}") for s in range(ADJ_RING)]
        out_stored = [sem(f"out_stored{s}") for s in range(2)]
        ident_zeroed = sem("ident_zeroed")
        ident_ready = sem("ident_ready")
        vt_ready = sem("vt_ready")
        vt_hi_done = sem("vt_hi_done")
        vt_lo_done = sem("vt_lo_done")
        v_hi_done = sem("v_hi_done")
        v_lo_done = sem("v_lo_done")
        stat_step = sem("stat_step")
        var_ready = sem("var_ready")
        std_ready = sem("std_ready")
        rstd_ready = sem("rstd_ready")
        moments_picked = sem("moments_picked")
        norm_done = sem("norm_done")
        ht_ready = sem("ht_ready")
        relu_done = sem("relu_done")
        q_ready = sem("q_ready")
        q_scaled = sem("q_scaled")
        q_lo_done = sem("q_lo_done")
        mask_ready = sem("mask_ready")
        scores_ready = sem("scores_ready")
        masked_done = sem("masked_done")
        max_ready = sem("max_ready")
        exp_done = sem("exp_done")
        pt_ready = sem("pt_ready")
        pt_hi_done = sem("pt_hi_done")
        pt_lo_done = sem("pt_lo_done")
        pv_done = sem("pv_done")
        sum_ready = sem("sum_ready")
        inv_ready = sem("inv_ready")
        part_ready = sem("part_ready")
        out_ready = sem("out_ready")

        waits_taken = {e: sem(f"waits_taken_{e.name}") for e in (mybir.EngineType.DVE, mybir.EngineType.Pool)}

        block = ctx.enter_context(nc.Block())

        def tile_behind(i, par, k, lag):
            t = STEPS + k - lag
            if t >= 0:
                return 2 * i + par - 1, (par + 1) % 2, t
            return 2 * i + par - 2, par, t + STEPS

        def exists(i, rb):
            return not isinstance(i, int) or 0 <= rb < RB

        def rows(i, par, shift=0):
            if isinstance(i, int):
                return slice((2 * i + par + shift) * P, (2 * i + par + shift + 1) * P)
            return bass.ds(i * (2 * P) + (par + shift) * P, P)

        def hold_sequencer(eng):
            eng.sem_inc(waits_taken[eng.engine], 1)

        @block.sync
        def _(sp):
            v_stage = probs[:, 1, :].rearrange("p (c d) -> p c d", d=D)
            x_stage = probs[:, 0, :].rearrange("p (c d) -> p c d", d=D)
            v_dram = inp.rearrange("(c p) d -> p c d", p=P)
            x_dram = x.rearrange("(c p) d -> p c d", p=P)
            cu = CH // UNITS
            for u in range(UNITS):
                sp.dma_start(v_stage[:, u * cu:(u + 1) * cu, :],
                             v_dram[:, u * cu:(u + 1) * cu, :]).then_inc(v_loaded[u], 16)
            hx = RB // 2
            for u in range(2):
                sp.dma_start(x_stage[:, u * hx:(u + 1) * hx, :],
                             x_dram[:, u * hx:(u + 1) * hx, :]).then_inc(x_loaded[u], 16)
            sp.dma_start(x_ln[:, 0, :], x[0:P, :]).then_inc(x_ln_loaded[0], 16)
            sp.dma_start(w_sb[:], weight).then_inc(w_loaded, 16)

            def row_block(i, par):
                r = 2 * i + par
                if exists(i, r):
                    for u in range(UNITS):
                        slot = (UNITS * par + u) % ADJ_RING
                        if not isinstance(i, int) or UNITS * r + u >= ADJ_RING:
                            sp.wait_ge(mask_ready, UNITS * r + u - ADJ_RING + 1)
                        sp.dma_start(adj_in[:, slot, :],
                                     adj[rows(i, par), u * UNIT:(u + 1) * UNIT]).then_inc(adj_loaded[slot], 16)
                        if u == 0 and exists(i, r + 1) and not (isinstance(i, int) and r + 1 >= RB):
                            if not isinstance(i, int) or r >= 1:
                                sp.wait_ge(norm_done, r)
                            load_x_ln(i, par)
                        if u == 2:
                            store_and_reload(i, par)
                else:
                    store_and_reload(i, par)

            def load_x_ln(i, par):
                sp.dma_start(x_ln[:, (par + 1) % 2, :],
                             x[rows(i, par, 1), :]).then_inc(x_ln_loaded[(par + 1) % 2], 16)

            def store_and_reload(i, par):
                r = 2 * i + par
                if exists(i, r - 3):
                    sp.wait_ge(out_ready, r - 2)
                    sp.dma_start(out[rows(i, par, -3), :],
                                 out_sb[:, (par + 1) % 2, :]).then_inc(out_stored[(par + 1) % 2], 16)
                if exists(i, r - 1):
                    sp.dma_start(x_res[:, (par + 1) % 2, :],
                                 x[rows(i, par, -1), :]).then_inc(x_res_loaded[(par + 1) % 2], 16)

            row_block(0, 0)
            row_block(0, 1)
            row_block(1, 0)
            row_block(1, 1)
            with sp.Fori(2, RB // 2 - 1) as i:
                row_block(i, 0)
                row_block(i, 1)
            row_block(RB // 2 - 1, 0)
            row_block(RB // 2 - 1, 1)
            row_block(RB // 2, 0)
            sp.wait_ge(out_ready, RB - 1)
            sp.dma_start(out[(RB - 2) * P:(RB - 1) * P, :], out_sb[:, 0, :]).then_inc(out_stored[0], 16)
            sp.wait_ge(out_ready, RB)
            sp.dma_start(out[(RB - 1) * P:RB * P, :], out_sb[:, 1, :]).then_inc(out_stored[1], 16)
            sp.wait_ge(out_stored[0], 16 * (RB // 2))
            sp.wait_ge(out_stored[1], 16 * (RB // 2))

        @block.gpsimd
        def _(pool):
            nc.gpsimd.memset(ident[:], 0.0).then_inc(ident_zeroed, 1)
            pool.wait_ge(ident_zeroed, 1)
            nc.gpsimd.affine_select(out=ident[:], in_=ident[:], compare_op=ALU.not_equal, fill=1.0,
                                    base=0, pattern=[[-1, P]], channel_multiplier=1).then_inc(ident_ready, 1)

            def normalise(b, par, first):
                if first:
                    pool.wait_ge(rstd_ready, 1)
                    cols = slice(0, 1)
                else:
                    pool.wait_ge(norm_done, b)
                    cols = bass.ds(b, 1)
                nc.gpsimd.tensor_copy(block_moments[:], moments[:, cols, :].rearrange("p a b -> p (a b)")
                                      ).then_inc(moments_picked, 1)
                pool.wait_ge(moments_picked, b + 1)
                if first:
                    pool.wait_ge(x_ln_loaded[0], 16)
                else:
                    pool.wait_ge(x_ln_loaded[par], load_count[0])
                    pool.wait_ge(ht_ready, b)
                hold_sequencer(pool)
                nc.gpsimd.tensor_scalar(h_norm[:], x_ln[:, par, :], block_moments[:, 0:1], block_moments[:, 1:2],
                                        ALU.subtract, ALU.mult).then_inc(norm_done, 1)

            load_count = [None]

            def split_q(b, par):
                pool.wait_ge(q_scaled, 2 * b + 2)
                nc.gpsimd.tensor_tensor(q_lo[:, par, :], q_full[:], q_hi[:, par, :].bitcast(F32),
                                        ALU.subtract).then_inc(q_lo_done, 1)

            def row_block(i, par):
                r = 2 * i + par
                if not exists(i, r):
                    return
                for u in range(UNITS):
                    slot = (UNITS * par + u) % ADJ_RING
                    pool.wait_ge(adj_loaded[slot], 16 * (i * (2 * UNITS // ADJ_RING) + (UNITS * par + u) // ADJ_RING + 1))
                    if not isinstance(i, int) or UNITS * r + u >= MASK_RING:
                        pool.wait_ge(masked_done, UNITS * r + u - MASK_RING + 1)
                    hold_sequencer(pool)
                    nc.gpsimd.tensor_scalar(mask_add[:, u % MASK_RING, :], adj_in[:, slot, :], 0.0, MASKED,
                                            ALU.is_le, ALU.mult).then_inc(mask_ready, 1)
                    if u == 0 and exists(i, r + 1):
                        load_count[0] = 16 * (i + 1 + par)
                        normalise(r + 1, (par + 1) % 2, False)
                    if u == UNITS - 1 and exists(i, r + 1):
                        split_q(r + 1, (par + 1) % 2)

            normalise(0, 0, True)
            split_q(0, 0)
            for u in range(UNITS):
                cu = CH // UNITS
                pool.wait_ge(v_hi_done, u + 1)
                nc.gpsimd.tensor_tensor(
                    v_hilo[:, u * cu:(u + 1) * cu, 1, :],
                    probs[:, 1, u * UNIT:(u + 1) * UNIT].rearrange("p (c d) -> p c d", d=D),
                    v_hilo[:, u * cu:(u + 1) * cu, 0, :].bitcast(F32), ALU.subtract).then_inc(v_lo_done, 1)
            row_block(0, 0)
            row_block(0, 1)
            with pool.Fori(1, RB // 2 - 1) as i:
                row_block(i, 0)
                row_block(i, 1)
            row_block(RB // 2 - 1, 0)
            row_block(RB // 2 - 1, 1)

        @block.tensor
        def _(pe):
            pe.wait_ge(ident_ready, 1)
            for u in range(UNITS):
                pe.wait_ge(v_loaded[u], 16)
                if u >= 2:
                    pe.wait_ge(vt_lo_done, u - 1)
                for c in range(UNIT // P):
                    last = nc.tensor.transpose(ps_scores[:, u % 2, c * P:(c + 1) * P],
                                               probs[:, 1, u * UNIT + c * P:u * UNIT + (c + 1) * P], ident[:])
                last.then_inc(vt_ready, 1)

            def transpose_h(b, par):
                if not isinstance(b, int) or b >= 3:
                    pe.wait_ge(out_ready, b - 2)
                pe.wait_ge(norm_done, b + 1)
                nc.tensor.transpose(ps_ht(par), h_norm[:], ident[:]).then_inc(ht_ready, 1)

            def project_q(b, par):
                pe.wait_ge(relu_done, b + 1)
                nc.tensor.matmul(ps_q(par), w_sb[:], h_t[:], start=True, stop=True).then_inc(q_ready, 1)

            def scores(i, par, k):
                r, u = 2 * i + par, k // 2
                if k == 0:
                    pe.wait_ge(q_lo_done, r + 1)
                if k % 2 == 0 and (not isinstance(i, int) or UNITS * r + u >= 2):
                    pe.wait_ge(masked_done, UNITS * r + u - 1)
                dst = ps_scores[:, u % 2, (k % 2) * BANK:(k % 2 + 1) * BANK]
                cols = slice(k * BANK, (k + 1) * BANK)
                nc.tensor.matmul(dst, q_hi[:, par, :], vt_hi[:, cols], start=True, stop=False)
                nc.tensor.matmul(dst, q_hi[:, par, :], vt_lo[:, cols], start=False, stop=False)
                last = nc.tensor.matmul(dst, q_lo[:, par, :], vt_hi[:, cols], start=False, stop=True)
                if k % 2 == 1:
                    last.then_inc(scores_ready, 1)

            def transpose_probs(rb, par, t):
                if t % 2 == 0:
                    pe.wait_ge(exp_done, UNITS * rb + t // 2 + 1)
                if not isinstance(rb, int) or STEPS * rb + t >= 2:
                    pe.wait_ge(pt_lo_done, STEPS * rb + t - 1)
                for c in range(CPS):
                    last = nc.tensor.transpose(ps_pt[:, t % 2, c * P:(c + 1) * P],
                                               probs[:, par, t * BANK + c * P:t * BANK + (c + 1) * P], ident[:])
                last.then_inc(pt_ready, 1)

            def times_v(rb, par, t):
                if t == 0 and (not isinstance(rb, int) or rb >= 2):
                    pe.wait_ge(out_ready, rb - 1)
                pe.wait_ge(pt_lo_done, STEPS * rb + t + 1)
                for c in range(CPS):
                    ch = t * CPS + c
                    cols = slice(c * P, (c + 1) * P)
                    nc.tensor.matmul(ps_out[:, par, 0:2 * D], pt_hi[:, t % PT_RING, cols], v_hilo[:, ch, :, :],
                                     start=(ch == 0), stop=False)
                    last = nc.tensor.matmul(ps_out[:, par, 0:D], pt_lo[:, t % PT_RING, cols], v_hilo[:, ch, 0, :],
                                            start=False, stop=(ch == CH - 1))
                last.then_inc(pv_done, 1)

            def row_block(i, par):
                r = 2 * i + par
                for k in range(STEPS):
                    if exists(i, r):
                        scores(i, par, k)
                    rb, tpar, t = tile_behind(i, par, k, T_LAG)
                    if exists(i, rb):
                        transpose_probs(rb, tpar, t)
                    if k == 7 and exists(i, r + 1):
                        transpose_h(r + 1, (par + 1) % 2)
                    if k == 9 and exists(i, r + 1):
                        project_q(r + 1, (par + 1) % 2)
                    rb, tpar, t = tile_behind(i, par, k, PV_LAG)
                    if exists(i, rb):
                        times_v(rb, tpar, t)

            transpose_h(0, 0)
            pe.wait_ge(w_loaded, 16)
            project_q(0, 0)
            pe.wait_ge(vt_lo_done, UNITS)
            row_block(0, 0)
            pe.wait_ge(v_lo_done, UNITS)
            row_block(0, 1)
            with pe.Fori(1, RB // 2 - 1) as i:
                row_block(i, 0)
                row_block(i, 1)
            row_block(RB // 2 - 1, 0)
            row_block(RB // 2 - 1, 1)
            row_block(RB // 2, 0)
            row_block(RB // 2, 1)

        @block.scalar
        def _(act):
            for u in range(UNITS):
                act.wait_ge(vt_ready, u + 1)
                nc.scalar.copy(vt_hi[:, u * UNIT:(u + 1) * UNIT], ps_scores[:, u % 2, :]).then_inc(vt_hi_done, 1)
            act.wait_ge(var_ready, 1)
            nc.scalar.activation(stat_b[:], stat_a[:], ACT.Sqrt).then_inc(std_ready, 1)

            def relu_h(b, par):
                act.wait_ge(ht_ready, b + 1)
                if not isinstance(b, int) or b >= 1:
                    act.wait_ge(q_ready, b)
                nc.scalar.activation(h_t[:], ps_ht(par), ACT.Relu).then_inc(relu_done, 1)

            def scale_q(b, par):
                act.wait_ge(q_ready, b + 1)
                if not isinstance(b, int) or b >= 1:
                    act.wait_ge(q_lo_done, b)
                nc.scalar.mul(q_full[:], ps_q(par), 1.0 / TEMPERATURE).then_inc(q_scaled, 1)
                if not isinstance(b, int) or b >= 2:
                    act.wait_ge(scores_ready, UNITS * b - UNITS)
                nc.scalar.mul(q_hi[:, par, :], ps_q(par), 1.0 / TEMPERATURE).then_inc(q_scaled, 1)

            def split_hi(rb, t):
                act.wait_ge(pt_ready, STEPS * rb + t + 1)
                if not isinstance(rb, int) or STEPS * rb + t >= PT_RING:
                    act.wait_ge(pv_done, STEPS * rb + t - PT_RING + 1)
                nc.scalar.copy(pt_hi[:, t % PT_RING, :], ps_pt[:, t % 2, :]).then_inc(pt_hi_done, 1)

            def exponent(rb, par, u):
                if u == 0:
                    act.wait_ge(max_ready, rb + 1)
                    if not isinstance(rb, int) or rb >= 2:
                        act.wait_ge(sum_ready, rb - 1)
                piece = probs[:, par, u * UNIT:(u + 1) * UNIT]
                nc.scalar.activation(piece, piece, ACT.Exp, bias=neg_max[:, par:par + 1], scale=1.0,
                                     accum_out=unit_sum[:, par, u:u + 1]).then_inc(exp_done, 1)

            def row_block(i, par):
                r = 2 * i + par
                for k in range(STEPS):
                    rb, _, t = tile_behind(i, par, k, T_LAG)
                    if exists(i, rb):
                        split_hi(rb, t)
                    if k % 2 == 0 and exists(i, r - 1):
                        exponent(r - 1, (par + 1) % 2, k // 2)
                    if k == 8 and exists(i, r + 1):
                        relu_h(r + 1, (par + 1) % 2)
                    if k == 10 and exists(i, r + 1):
                        scale_q(r + 1, (par + 1) % 2)

            relu_h(0, 0)
            scale_q(0, 0)
            for u in range(UNITS):
                cu = CH // UNITS
                act.wait_ge(v_loaded[u], 16)
                nc.scalar.copy(v_hilo[:, u * cu:(u + 1) * cu, 0, :],
                               probs[:, 1, u * UNIT:(u + 1) * UNIT].rearrange("p (c d) -> p c d", d=D)
                               ).then_inc(v_hi_done, 1)
            row_block(0, 0)
            row_block(0, 1)
            with act.Fori(1, RB // 2 - 1) as i:
                row_block(i, 0)
                row_block(i, 1)
            row_block(RB // 2 - 1, 0)
            row_block(RB // 2 - 1, 1)
            row_block(RB // 2, 0)
            row_block(RB // 2, 1)

        @block.vector
        def _(dve):
            for u in range(UNITS):
                dve.wait_ge(vt_hi_done, u + 1)
                cols = slice(u * UNIT, (u + 1) * UNIT)
                nc.vector.tensor_tensor(vt_lo[:, cols], ps_scores[:, u % 2, :], vt_hi[:, cols].bitcast(F32),
                                        ALU.subtract).then_inc(vt_lo_done, 1)
            for b in range(RB):
                if b % (RB // 2) == 0:
                    dve.wait_ge(x_loaded[b // (RB // 2)], 16)
                last = nc.vector.bn_stats(stats[:, b, :], probs[:, 0, b * D:(b + 1) * D])
            last.then_inc(stat_step, 1)
            dve.wait_ge(stat_step, 1)
            mean_even, mean_odd = stats[:, :, 1], stats[:, :, 4]
            nc.vector.tensor_tensor(moments[:, :, 0], mean_even, mean_odd, ALU.add)
            nc.vector.tensor_tensor(stat_a[:], mean_even, mean_odd, ALU.subtract)
            nc.vector.tensor_tensor(stat_b[:], stats[:, :, 2], stats[:, :, 5], ALU.add).then_inc(stat_step, 1)
            dve.wait_ge(stat_step, 2)
            nc.vector.tensor_scalar(moments[:, :, 0], moments[:, :, 0], 0.5, None, ALU.mult)
            nc.vector.tensor_tensor(stat_a[:], stat_a[:], stat_a[:], ALU.mult)
            nc.vector.tensor_scalar(stat_b[:], stat_b[:], 1.0 / D, EPS, ALU.mult, ALU.add).then_inc(stat_step, 1)
            dve.wait_ge(stat_step, 3)
            nc.vector.scalar_tensor_tensor(out=stat_a[:], in0=stat_a[:], scalar=0.25, in1=stat_b[:],
                                           op0=ALU.mult, op1=ALU.add).then_inc(var_ready, 1)
            dve.wait_ge(std_ready, 1)
            nc.vector.reciprocal(moments[:, :, 1], stat_b[:]).then_inc(rstd_ready, 1)

            def add_mask(i, par, u):
                r = 2 * i + par
                dve.wait_ge(scores_ready, UNITS * r + u + 1)
                dve.wait_ge(mask_ready, UNITS * r + u + 1)
                if not isinstance(i, int) or r >= 2:
                    dve.wait_ge(pt_ready, STEPS * (r - 2) + 2 * u + 2)
                hold_sequencer(dve)
                nc.vector.tensor_tensor_reduce(
                    out=probs[:, par, u * UNIT:(u + 1) * UNIT], in0=ps_scores[:, u % 2, :],
                    in1=mask_add[:, u % MASK_RING, :], scale=1.0, scalar=LOWEST, op0=ALU.add, op1=ALU.max,
                    accum_out=unit_max[:, par, u:u + 1]).then_inc(masked_done, 1)

            def row_max(i, par):
                r = 2 * i + par
                dve.wait_ge(masked_done, UNITS * r + UNITS)
                if not isinstance(i, int) or r >= 2:
                    dve.wait_ge(exp_done, UNITS * (r - 1))
                nc.vector.tensor_reduce(neg_max[:, par:par + 1], unit_max[:, par, :], AX_X, ALU.max,
                                        negate=True).then_inc(max_ready, 1)

            def split_lo(rb, t):
                dve.wait_ge(pt_hi_done, STEPS * rb + t + 1)
                nc.vector.tensor_tensor(pt_lo[:, t % PT_RING, :], ps_pt[:, t % 2, :],
                                        pt_hi[:, t % PT_RING, :].bitcast(F32), ALU.subtract).then_inc(pt_lo_done, 1)

            def invert_sum(rb, par):
                dve.wait_ge(exp_done, UNITS * rb + UNITS)
                nc.vector.reduce_sum(row_sum[:, par:par + 1], unit_sum[:, par, :], AX_X).then_inc(sum_ready, 1)
                dve.wait_ge(sum_ready, rb + 1)
                nc.vector.reciprocal(inv_sum[:, par:par + 1], row_sum[:, par:par + 1]).then_inc(inv_ready, 1)

            def finish(i, rb, par):
                dve.wait_ge(pv_done, STEPS * rb + STEPS)
                dve.wait_ge(inv_ready, rb + 1)
                dve.wait_ge(x_res_loaded[par], 16 * i)
                nc.vector.scalar_tensor_tensor(out=out_part[:], in0=ps_out[:, par, D:2 * D],
                                               scalar=inv_sum[:, par:par + 1], in1=x_res[:, par, :],
                                               op0=ALU.mult, op1=ALU.add).then_inc(part_ready, 1)
                dve.wait_ge(part_ready, rb + 1)
                if not isinstance(i, int) or rb >= 2:
                    dve.wait_ge(out_stored[par], 16 * (i - 1))
                nc.vector.scalar_tensor_tensor(out=out_sb[:, par, :], in0=ps_out[:, par, 0:D],
                                               scalar=inv_sum[:, par:par + 1], in1=out_part[:],
                                               op0=ALU.mult, op1=ALU.add).then_inc(out_ready, 1)

            def row_block(i, par):
                r = 2 * i + par
                for k in range(STEPS):
                    rb, _, t = tile_behind(i, par, k, T_LAG)
                    if exists(i, rb):
                        split_lo(rb, t)
                    if k % 2 == 1 and exists(i, r):
                        add_mask(i, par, k // 2)
                    if k == 2 and exists(i, r - 2):
                        invert_sum(r - 2, par)
                    if k == 5 and exists(i, r - 2):
                        finish(i, r - 2, par)
                if exists(i, r):
                    row_max(i, par)

            row_block(0, 0)
            dve.wait_ge(v_lo_done, UNITS)
            row_block(0, 1)
            with dve.Fori(1, RB // 2 - 1) as i:
                row_block(i, 0)
                row_block(i, 1)
            row_block(RB // 2 - 1, 0)
            row_block(RB // 2 - 1, 1)
            row_block(RB // 2, 0)
            row_block(RB // 2, 1)


def kernel(x, adj, L0_gnn_input, L0_gnn_weight):
    import numpy as np
    import concourse.bacc as bacc
    from concourse.bass_utils import run_bass_kernel_spmd

    nc = bacc.Bacc("TRN2", target_bir_lowering=False, num_devices=1)
    arrays, args = {}, []
    for name, a in (("x", x), ("adj", adj), ("v", L0_gnn_input), ("w", L0_gnn_weight)):
        a = np.ascontiguousarray(a)
        arrays[name] = a
        args.append(nc.dram_tensor(name, a.shape, mybir.dt.from_np(a.dtype), kind="ExternalInput").ap())
    y = nc.dram_tensor("y", x.shape, mybir.dt.float32, kind="ExternalOutput").ap()
    gnn_attention(nc, *args, y)
    r = run_bass_kernel_spmd(nc, [arrays], core_ids=[0])
    return r.results[0]["y"]
```

```python
from contextlib import ExitStack

import concourse.bass as bass
from concourse import mybir

ALU = mybir.AluOpType
ACT = mybir.ActivationFunctionType
AX_X = mybir.AxisListType.X
F32 = mybir.dt.float32
F32R = mybir.dt.float32r
I32 = mybir.dt.int32

P = 128
BANK = 512
UNIT = 2 * BANK
TILE = BANK // 2
TEMPERATURE = 0.07
EPS = 1e-5
MASKED = -(2.0 ** 100)
LOWEST = -3.0e38

ADJ_RING = 4
PT_RING = 4


def gnn_attention(nc, x, adj, inp, weight, out):
    M, D = x.shape
    N = inp.shape[0]
    RB = M // P
    PAIRS = RB // 2
    UNITS = N // UNIT
    STEPS = 2 * N // BANK
    HALF = STEPS // 2
    CH_TILE = TILE // P
    TPU = UNIT // TILE
    T_LAG = STEPS + 2
    PV_LAG = T_LAG + 2
    COPY_AT = PV_LAG - STEPS + 1
    TURN_AT = COPY_AT + 2
    FINISH_AT = TURN_AT + 2
    assert D == P and PAIRS % 2 == 0 and PAIRS >= 6 and N % UNIT == 0 and N // TILE == STEPS
    assert STEPS % PT_RING == 0 and 2 * UNITS % ADJ_RING == 0 and UNITS % 2 == 0

    with ExitStack() as ctx:
        def sb(name, shape, dt):
            return ctx.enter_context(nc.sbuf_tensor(name, shape, dt))

        def psum(name, shape, dt):
            return ctx.enter_context(nc.psum_tensor(name, shape, dt))

        def sem(name):
            return ctx.enter_context(nc.semaphore(name))

        v_hi = sb("v_hi", [P, N], F32R)
        v_lo = sb("v_lo", [P, N], F32R)
        vt_hi = sb("vt_hi", [P, N], F32R)
        vt_lo = sb("vt_lo", [P, N], F32R)
        probs_a = sb("probs_a", [P, 2, N], F32)
        probs_b = sb("probs_b", [P, N + UNIT], F32)
        adj_in = sb("adj_in", [P, ADJ_RING, UNIT], I32)
        pt_hi = sb("pt_hi", [P, PT_RING, CH_TILE, 2, P], F32R)
        pt_lo = sb("pt_lo", [P, PT_RING, CH_TILE, 2, P], F32R)
        w_sb = sb("w_sb", [P, D], F32)
        ident = sb("ident", [P, P], F32)
        x_ln = sb("x_ln", [P, 2, D], F32)
        x_res = sb("x_res", [P, 2, D], F32)
        h_norm = sb("h_norm", [P, 2, D], F32)
        h_t = sb("h_t", [P, 2 * P], F32)
        q_full = sb("q_full", [P, 2 * P], F32)
        q_hi = sb("q_hi", [P, 2, 2 * P], F32R)
        q_lo = sb("q_lo", [P, 2, 2 * P], F32R)
        stats = sb("stats", [P, RB, 6], F32)
        moments = sb("moments", [P, RB, 2], F32)
        pair_moments = sb("pair_moments", [P, 2, 2], F32)
        stat_a = sb("stat_a", [P, RB], F32)
        stat_b = sb("stat_b", [P, RB], F32)
        unit_max = sb("unit_max", [P, 2, UNITS], F32)
        neg_max = sb("neg_max", [P, 2], F32)
        unit_sum = sb("unit_sum", [P, 2, UNITS], F32)
        row_sum = sb("row_sum", [P, 2], F32)
        inv_sum = sb("inv_sum", [P, 2, 2], F32)
        out_t = sb("out_t", [P, 2 * P], F32)
        out_sb = sb("out_sb", [P, 2, D], F32)

        ps_scores = psum("ps_scores", [P, 2, UNIT], F32)
        ps_pt = psum("ps_pt", [P, 2, CH_TILE, 2, P], F32)
        ps_out = psum("ps_out", [P, 2, 2, 2 * P], F32)

        v_loaded = [sem(f"v_loaded{u}") for u in range(UNITS)]
        x_staged = sem("x_staged")
        w_loaded = sem("w_loaded")
        x_ln_loaded = sem("x_ln_loaded")
        x_res_loaded = sem("x_res_loaded")
        adj_loaded = [sem(f"adj_loaded{s}") for s in range(ADJ_RING)]
        out_stored = sem("out_stored")
        ident_zeroed = sem("ident_zeroed")
        ident_ready = sem("ident_ready")
        vt_ready = sem("vt_ready")
        vt_hi_done = sem("vt_hi_done")
        vt_lo_done = sem("vt_lo_done")
        v_hi_done = sem("v_hi_done")
        v_lo_done = sem("v_lo_done")
        stat_step = sem("stat_step")
        var_ready = sem("var_ready")
        std_ready = sem("std_ready")
        moments_ready = sem("moments_ready")
        moments_picked = sem("moments_picked")
        norm_done = sem("norm_done")
        ht_ready = sem("ht_ready")
        relu_done = sem("relu_done")
        q_ready = sem("q_ready")
        q_scaled = sem("q_scaled")
        q_lo_done = sem("q_lo_done")
        mask_ready = sem("mask_ready")
        scores_ready = sem("scores_ready")
        masked_done = sem("masked_done")
        max_ready = sem("max_ready")
        exp_done = [sem("exp_a_done"), sem("exp_b_done")]
        pt_ready = sem("pt_ready")
        pt_hi_done = sem("pt_hi_done")
        pt_lo_done = sem("pt_lo_done")
        pv_done = sem("pv_done")
        sum_ready = sem("sum_ready")
        inv_ready = sem("inv_ready")
        out_t_copied = sem("out_t_copied")
        out_turned = sem("out_turned")
        out_ready = sem("out_ready")
        waits_taken = {e: sem(f"waits_taken_{e.name}") for e in (mybir.EngineType.DVE, mybir.EngineType.Pool)}

        block = ctx.enter_context(nc.Block())

        def tile_behind(i, par, g, lag):
            t = STEPS + g - lag
            if t >= 0:
                return 2 * i + par - 1, (par + 1) % 2, t
            return 2 * i + par - 2, par, t + STEPS

        def exists(i, j):
            return not isinstance(i, int) or 0 <= j < PAIRS

        def later(i, n, least):
            return not isinstance(i, int) or n >= least

        def run_pairs(eng, pair):
            pair(0, 0)
            pair(0, 1)
            with eng.Fori(1, PAIRS // 2 - 1) as i:
                pair(i, 0)
                pair(i, 1)
            pair(PAIRS // 2 - 1, 0)
            pair(PAIRS // 2 - 1, 1)

        def rows(i, par, shift=0, n=2):
            first = int((par + shift) * 2 * P)
            return bass.ds(i * (4 * P) + first, n * P)

        def probs(b, par, col, n):
            if b == 0:
                return probs_a[:, par, col:col + n]
            if col >= N - UNIT:
                col += par * UNIT
            return probs_b[:, col:col + n]

        def hold_sequencer(eng):
            eng.sem_inc(waits_taken[eng.engine], 1)

        v_stage = probs_b[:, 0:N]
        x_stage = probs_a[:, 1, :]

        @block.sync
        def _(sp):
            def load_x_ln(i, par, shift):
                sp.dma_start(x_ln[:], x[rows(i, par, shift), :].rearrange("(b p) d -> p b d", p=P)
                             ).then_inc(x_ln_loaded, 16)

            load_x_ln(0, 0, 0)
            v_dram = inp.rearrange("(c p) d -> p c d", p=P)
            cu = UNIT // P
            for u in range(UNITS):
                sp.dma_start(v_stage[:, u * UNIT:(u + 1) * UNIT].rearrange("p (c d) -> p c d", d=D),
                             v_dram[:, u * cu:(u + 1) * cu, :]).then_inc(v_loaded[u], 16)
                if u == 0:
                    sp.dma_start(w_sb[:], weight).then_inc(w_loaded, 16)

            def pair(i, par):
                j = 2 * i + par
                for n in range(2 * UNITS):
                    b, u = n // UNITS, n % UNITS
                    slot = n % ADJ_RING
                    if later(i, 2 * UNITS * j + n, ADJ_RING):
                        sp.wait_ge(masked_done, 2 * UNITS * j + n - ADJ_RING + 1)
                    sp.dma_start(adj_in[:, slot, :],
                                 adj[rows(i, par, b / 2, 1), u * UNIT:(u + 1) * UNIT]).then_inc(adj_loaded[slot], 16)
                    if n == 1 and isinstance(i, int) and j == 0:
                        sp.dma_start(x_stage.rearrange("p (c d) -> p c d", d=D),
                                     x.rearrange("(c p) d -> p c d", p=P)).then_inc(x_staged, 16)
                    if n == 2 and exists(i, j + 1):
                        sp.wait_ge(norm_done, j + 1)
                        load_x_ln(i, par, 1)
                    if n == 2 * UNITS - 2:
                        store_and_reload(i, par)

            def store_and_reload(i, par):
                j = 2 * i + par
                if exists(i, j - 2):
                    sp.wait_ge(out_ready, j - 1)
                    sp.dma_start(out[rows(i, par, -2), :].rearrange("(b p) d -> p b d", p=P), out_sb[:]
                                 ).then_inc(out_stored, 16)
                if exists(i, j - 1):
                    sp.dma_start(x_res[:], x[rows(i, par, -1), :].rearrange("(b p) d -> p b d", p=P)
                                 ).then_inc(x_res_loaded, 16)

            run_pairs(sp, pair)
            store_and_reload(PAIRS // 2, 0)
            store_and_reload(PAIRS // 2, 1)
            sp.wait_ge(out_stored, 16 * PAIRS)

        @block.gpsimd
        def _(pool):
            nc.gpsimd.memset(ident[:], 0.0).then_inc(ident_zeroed, 1)
            pool.wait_ge(ident_zeroed, 1)
            nc.gpsimd.affine_select(out=ident[:], in_=ident[:], compare_op=ALU.not_equal, fill=1.0,
                                    base=0, pattern=[[-1, P]], channel_multiplier=1).then_inc(ident_ready, 1)

            def normalise(j, cols):
                if later(j, j, 1):
                    pool.wait_ge(norm_done, j)
                nc.gpsimd.tensor_copy(pair_moments[:], moments[:, cols, :]).then_inc(moments_picked, 1)
                pool.wait_ge(moments_picked, j + 1)
                pool.wait_ge(x_ln_loaded, 16 * (j + 1))
                if later(j, j, 1):
                    pool.wait_ge(ht_ready, j)
                hold_sequencer(pool)
                for b in range(2):
                    last = nc.gpsimd.tensor_scalar(h_norm[:, b, :], x_ln[:, b, :], pair_moments[:, b, 0:1],
                                                   pair_moments[:, b, 1:2], ALU.subtract, ALU.mult)
                last.then_inc(norm_done, 1)

            def split_q(j, par):
                pool.wait_ge(q_scaled, 2 * j + 2)
                nc.gpsimd.tensor_tensor(q_lo[:, par, :], q_full[:], q_hi[:, par, :].bitcast(F32),
                                        ALU.subtract).then_inc(q_lo_done, 1)

            pool.wait_ge(moments_ready, 1)
            normalise(0, slice(0, 2))
            split_q(0, 0)
            for u in range(UNITS):
                cols = slice(u * UNIT, (u + 1) * UNIT)
                pool.wait_ge(v_hi_done, u + 1)
                nc.gpsimd.tensor_tensor(v_lo[:, cols], v_stage[:, cols], v_hi[:, cols].bitcast(F32),
                                        ALU.subtract).then_inc(v_lo_done, 1)
            pool.wait_ge(moments_ready, 2)

            def pair(i, par):
                j = 2 * i + par
                if exists(i, j + 1):
                    normalise(j + 1, bass.ds(i * 4 + (par + 1) * 2, 2))
                    split_q(j + 1, (par + 1) % 2)

            run_pairs(pool, pair)

        @block.tensor
        def _(pe):
            def transpose_h(j, par):
                pe.wait_ge(norm_done, j + 1)
                if later(j, j, 3):
                    pe.wait_ge(out_ready, j - 2)
                for b in range(2):
                    last = nc.tensor.transpose(ps_out[:, (par + 1) % 2, 0, b * P:(b + 1) * P], h_norm[:, b, :],
                                               ident[:])
                last.then_inc(ht_ready, 1)

            def project_q(j, par):
                pe.wait_ge(relu_done, j + 1)
                nc.tensor.matmul(ps_out[:, (par + 1) % 2, 1, :], w_sb[:], h_t[:], start=True, stop=True
                                 ).then_inc(q_ready, 1)

            def scores(i, par, g):
                j, b, k = 2 * i + par, g // HALF, g % HALF
                unit = 2 * UNITS * j + g // 2
                if g == 0:
                    pe.wait_ge(q_lo_done, j + 1)
                if g % 2 == 0 and later(i, unit, 2):
                    pe.wait_ge(masked_done, unit - 1)
                dst = ps_scores[:, (g // 2) % 2, (g % 2) * BANK:(g % 2 + 1) * BANK]
                cols = slice(k * BANK, (k + 1) * BANK)
                q = slice(b * P, (b + 1) * P)
                nc.tensor.matmul(dst, q_hi[:, par, q], vt_hi[:, cols], start=True, stop=False)
                nc.tensor.matmul(dst, q_hi[:, par, q], vt_lo[:, cols], start=False, stop=False)
                last = nc.tensor.matmul(dst, q_lo[:, par, q], vt_hi[:, cols], start=False, stop=True)
                if g % 2 == 1:
                    last.then_inc(scores_ready, 1)

            def transpose_probs(j, par, t):
                if t % TPU == 0:
                    pe.wait_ge(exp_done[0], UNITS * j + t // TPU + 1)
                    pe.wait_ge(exp_done[1], UNITS * j + t // TPU + 1)
                if later(j, STEPS * j + t, 2):
                    pe.wait_ge(pt_lo_done, STEPS * j + t - 1)
                for c in range(CH_TILE):
                    for b in range(2):
                        last = nc.tensor.transpose(ps_pt[:, t % 2, c, b, :], probs(b, par, t * TILE + c * P, P),
                                                   ident[:])
                last.then_inc(pt_ready, 1)

            def times_v(j, par, t):
                if t == 0 and later(j, j, 2):
                    pe.wait_ge(out_ready, j - 1)
                pe.wait_ge(pt_lo_done, STEPS * j + t + 1)
                acc = ps_out[:, par, 0, :]
                for c in range(CH_TILE):
                    ch = t * CH_TILE + c
                    v = slice(ch * P, (ch + 1) * P)
                    hi = pt_hi[:, t % PT_RING, c, :, :].rearrange("p b m -> p (b m)")
                    lo = pt_lo[:, t % PT_RING, c, :, :].rearrange("p b m -> p (b m)")
                    nc.tensor.matmul(acc, v_hi[:, v], hi, start=(ch == 0), stop=False)
                    nc.tensor.matmul(acc, v_lo[:, v], hi, start=False, stop=False)
                    last = nc.tensor.matmul(acc, v_hi[:, v], lo, start=False, stop=(ch == N // P - 1))
                last.then_inc(pv_done, 1)

            def turn_out(j, par):
                pe.wait_ge(out_t_copied, j + 1)
                for b in range(2):
                    last = nc.tensor.transpose(ps_out[:, par, 1, b * P:(b + 1) * P], out_t[:, b * P:(b + 1) * P],
                                               ident[:])
                last.then_inc(out_turned, 1)

            def pair(i, par):
                j = 2 * i + par
                for g in range(STEPS):
                    if exists(i, j):
                        scores(i, par, g)
                    tj, tpar, t = tile_behind(i, par, g, T_LAG)
                    if exists(i, tj):
                        transpose_probs(tj, tpar, t)
                    tj, tpar, t = tile_behind(i, par, g, PV_LAG)
                    if exists(i, tj):
                        times_v(tj, tpar, t)
                    if g == TURN_AT and exists(i, j - 2):
                        turn_out(j - 2, par)
                    if g == HALF and exists(i, j + 1):
                        transpose_h(j + 1, (par + 1) % 2)
                    if g == HALF + 2 and exists(i, j + 1):
                        project_q(j + 1, (par + 1) % 2)

            pe.wait_ge(ident_ready, 1)
            transpose_h(0, 0)
            pe.wait_ge(w_loaded, 16)
            project_q(0, 0)
            for u in range(UNITS):
                pe.wait_ge(v_loaded[u], 16)
                if u >= 2:
                    pe.wait_ge(vt_lo_done, u - 1)
                for c in range(UNIT // P):
                    last = nc.tensor.transpose(ps_scores[:, u % 2, c * P:(c + 1) * P],
                                               v_stage[:, u * UNIT + c * P:u * UNIT + (c + 1) * P], ident[:])
                last.then_inc(vt_ready, 1)
            pe.wait_ge(vt_lo_done, UNITS)
            pair(0, 0)
            pe.wait_ge(v_lo_done, UNITS)
            pair(0, 1)
            with pe.Fori(1, PAIRS // 2 - 1) as i:
                pair(i, 0)
                pair(i, 1)
            pair(PAIRS // 2 - 1, 0)
            pair(PAIRS // 2 - 1, 1)
            pair(PAIRS // 2, 0)
            pair(PAIRS // 2, 1)

        @block.scalar
        def _(act):
            def deviation(n, cols):
                act.wait_ge(var_ready, n)
                nc.scalar.activation(stat_b[:, cols], stat_a[:, cols], ACT.Sqrt).then_inc(std_ready, 1)

            def relu_h(j, par):
                act.wait_ge(ht_ready, j + 1)
                if later(j, j, 1):
                    act.wait_ge(q_ready, j)
                nc.scalar.activation(h_t[:], ps_out[:, (par + 1) % 2, 0, :], ACT.Relu).then_inc(relu_done, 1)

            def scale_q(j, par):
                q = ps_out[:, (par + 1) % 2, 1, :]
                act.wait_ge(q_ready, j + 1)
                if later(j, j, 1):
                    act.wait_ge(q_lo_done, j)
                nc.scalar.mul(q_full[:], q, 1.0 / TEMPERATURE).then_inc(q_scaled, 1)
                if later(j, j, 2):
                    act.wait_ge(scores_ready, 2 * UNITS * (j - 1))
                nc.scalar.mul(q_hi[:, par, :], q, 1.0 / TEMPERATURE).then_inc(q_scaled, 1)

            def split_hi(j, t):
                act.wait_ge(pt_ready, STEPS * j + t + 1)
                if later(j, STEPS * j + t, PT_RING):
                    act.wait_ge(pv_done, STEPS * j + t - PT_RING + 1)
                nc.scalar.copy(pt_hi[:, t % PT_RING], ps_pt[:, t % 2]).then_inc(pt_hi_done, 1)

            def exponent(j, par, b, u):
                if u == 0:
                    act.wait_ge(max_ready, 2 * j + b + 1)
                    if later(j, j, 1):
                        act.wait_ge(sum_ready, 2 * j + b - 1)
                piece = probs(b, par, u * UNIT, UNIT)
                nc.scalar.activation(piece, piece, ACT.Exp, bias=neg_max[:, b:b + 1], scale=1.0,
                                     accum_out=unit_sum[:, b, u:u + 1]).then_inc(exp_done[b], 1)

            def copy_out_t(j, par):
                act.wait_ge(pv_done, STEPS * (j + 1))
                if later(j, j, 1):
                    act.wait_ge(out_turned, j)
                nc.scalar.copy(out_t[:], ps_out[:, par, 0, :]).then_inc(out_t_copied, 1)

            def pair(i, par):
                j = 2 * i + par
                for g in range(STEPS):
                    tj, _, t = tile_behind(i, par, g, T_LAG)
                    if exists(i, tj):
                        split_hi(tj, t)
                    if g % TPU == 0 and exists(i, j - 1):
                        exponent(j - 1, (par + 1) % 2, 1, g // TPU)
                    if g % TPU == 2:
                        u = (g - HALF) // TPU
                        if u >= 0 and exists(i, j):
                            exponent(j, par, 0, u)
                        if u < 0 and exists(i, j - 1):
                            exponent(j - 1, (par + 1) % 2, 0, u + UNITS)
                    if g == COPY_AT and exists(i, j - 2):
                        copy_out_t(j - 2, par)
                    if g == HALF + 1 and exists(i, j + 1):
                        relu_h(j + 1, (par + 1) % 2)
                    if g == HALF + 3 and exists(i, j + 1):
                        scale_q(j + 1, (par + 1) % 2)

            deviation(1, slice(0, 2))
            relu_h(0, 0)
            scale_q(0, 0)
            for u in range(UNITS):
                cols = slice(u * UNIT, (u + 1) * UNIT)
                act.wait_ge(vt_ready, u + 1)
                nc.scalar.copy(vt_hi[:, cols], ps_scores[:, u % 2, :]).then_inc(vt_hi_done, 1)
                nc.scalar.copy(v_hi[:, cols], v_stage[:, cols]).then_inc(v_hi_done, 1)
            deviation(2, slice(2, RB))
            run_pairs(act, pair)
            pair(PAIRS // 2, 0)
            pair(PAIRS // 2, 1)

        @block.vector
        def _(dve):
            def moments_of(n, blocks, source):
                for b in range(*blocks):
                    last = nc.vector.bn_stats(stats[:, b, :], source(b))
                last.then_inc(stat_step, 1)
                dve.wait_ge(stat_step, 3 * n - 2)
                cols = slice(*blocks)
                mean, a, b = moments[:, cols, 0], stat_a[:, cols], stat_b[:, cols]
                mean_even, mean_odd = stats[:, cols, 1], stats[:, cols, 4]
                nc.vector.tensor_tensor(mean, mean_even, mean_odd, ALU.add)
                nc.vector.tensor_tensor(a, mean_even, mean_odd, ALU.subtract)
                nc.vector.tensor_tensor(b, stats[:, cols, 2], stats[:, cols, 5], ALU.add).then_inc(stat_step, 1)
                dve.wait_ge(stat_step, 3 * n - 1)
                nc.vector.tensor_scalar(mean, mean, 0.5, None, ALU.mult)
                nc.vector.tensor_tensor(a, a, a, ALU.mult)
                nc.vector.tensor_scalar(b, b, 1.0 / D, EPS, ALU.mult, ALU.add).then_inc(stat_step, 1)
                dve.wait_ge(stat_step, 3 * n)
                nc.vector.scalar_tensor_tensor(out=a, in0=a, scalar=0.25, in1=b,
                                               op0=ALU.mult, op1=ALU.add).then_inc(var_ready, 1)

            def invert_deviation(n, cols):
                dve.wait_ge(std_ready, n)
                nc.vector.reciprocal(moments[:, cols, 1], stat_b[:, cols]).then_inc(moments_ready, 1)

            def make_mask(i, par, n):
                slot, per_pair = n % ADJ_RING, 2 * UNITS // ADJ_RING
                dve.wait_ge(adj_loaded[slot], 16 * (i * (2 * per_pair) + par * per_pair + n // ADJ_RING + 1))
                nc.vector.tensor_scalar(adj_in[:, slot, :].bitcast(F32), adj_in[:, slot, :], 0.0, MASKED,
                                        ALU.is_le, ALU.mult).then_inc(mask_ready, 1)

            def add_mask(i, par, n):
                j, b, u = 2 * i + par, n // UNITS, n % UNITS
                unit = 2 * UNITS * j + n
                dve.wait_ge(scores_ready, unit + 1)
                dve.wait_ge(mask_ready, unit + 1)
                back = 1 if b == 1 and u < UNITS - 1 else 2
                if later(i, j, back):
                    dve.wait_ge(pt_ready, STEPS * (j - back) + TPU * (u + 1))
                hold_sequencer(dve)
                nc.vector.tensor_tensor_reduce(
                    out=probs(b, par, u * UNIT, UNIT), in0=ps_scores[:, n % 2, :],
                    in1=adj_in[:, n % ADJ_RING, :].bitcast(F32), scale=1.0, scalar=LOWEST,
                    op0=ALU.add, op1=ALU.max, accum_out=unit_max[:, b, u:u + 1]).then_inc(masked_done, 1)

            def row_max(i, par, b):
                j = 2 * i + par
                dve.wait_ge(masked_done, UNITS * (2 * j + b + 1))
                if later(i, j, 1):
                    dve.wait_ge(exp_done[b], UNITS * j)
                nc.vector.tensor_reduce(neg_max[:, b:b + 1], unit_max[:, b, :], AX_X, ALU.max,
                                        negate=True).then_inc(max_ready, 1)

            def split_lo(j, t):
                dve.wait_ge(pt_hi_done, STEPS * j + t + 1)
                nc.vector.tensor_tensor(pt_lo[:, t % PT_RING], ps_pt[:, t % 2],
                                        pt_hi[:, t % PT_RING].bitcast(F32), ALU.subtract).then_inc(pt_lo_done, 1)

            def invert_sum(j, par, b):
                dve.wait_ge(exp_done[b], UNITS * (j + 1))
                nc.vector.reduce_sum(row_sum[:, b:b + 1], unit_sum[:, b, :], AX_X).then_inc(sum_ready, 1)
                dve.wait_ge(sum_ready, 2 * j + b + 1)
                nc.vector.reciprocal(inv_sum[:, par, b:b + 1], row_sum[:, b:b + 1]).then_inc(inv_ready, 1)

            def finish(j, par):
                dve.wait_ge(out_turned, j + 1)
                dve.wait_ge(inv_ready, 2 * j + 2)
                dve.wait_ge(x_res_loaded, 16 * (j + 1))
                if later(j, j, 1):
                    dve.wait_ge(out_stored, 16 * j)
                for b in range(2):
                    last = nc.vector.scalar_tensor_tensor(
                        out=out_sb[:, b, :], in0=ps_out[:, par, 1, b * P:(b + 1) * P],
                        scalar=inv_sum[:, par, b:b + 1], in1=x_res[:, b, :], op0=ALU.mult, op1=ALU.add)
                last.then_inc(out_ready, 1)

            def pair(i, par):
                j = 2 * i + par
                for g in range(STEPS):
                    if g % 2 == 0 and exists(i, j):
                        make_mask(i, par, g // 2)
                    tj, _, t = tile_behind(i, par, g, T_LAG)
                    if exists(i, tj):
                        split_lo(tj, t)
                    if g % 2 == 1 and exists(i, j):
                        add_mask(i, par, g // 2)
                        if g % HALF == HALF - 1:
                            row_max(i, par, g // HALF)
                    if g == FINISH_AT and exists(i, j - 2):
                        finish(j - 2, par)
                    if g == HALF and exists(i, j - 1):
                        invert_sum(j - 1, (par + 1) % 2, 0)
                    if g == STEPS - 2 and exists(i, j - 1):
                        invert_sum(j - 1, (par + 1) % 2, 1)

            dve.wait_ge(x_ln_loaded, 16)
            moments_of(1, (0, 2), lambda b: x_ln[:, b, :])
            invert_deviation(1, slice(0, 2))
            for u in range(UNITS):
                cols = slice(u * UNIT, (u + 1) * UNIT)
                dve.wait_ge(vt_hi_done, u + 1)
                nc.vector.tensor_tensor(vt_lo[:, cols], ps_scores[:, u % 2, :], vt_hi[:, cols].bitcast(F32),
                                        ALU.subtract).then_inc(vt_lo_done, 1)
            dve.wait_ge(x_staged, 16)
            moments_of(2, (2, RB), lambda b: x_stage[:, b * D:(b + 1) * D])
            invert_deviation(2, slice(2, RB))
            dve.wait_ge(v_lo_done, UNITS)
            run_pairs(dve, pair)
            pair(PAIRS // 2, 0)
            pair(PAIRS // 2, 1)


def kernel(x, adj, L0_gnn_input, L0_gnn_weight):
    import numpy as np
    import concourse.bacc as bacc
    from concourse.bass_utils import run_bass_kernel_spmd

    nc = bacc.Bacc("TRN2", target_bir_lowering=False, num_devices=1, dynamic_dma_scratch_size=1024)
    arrays, args = {}, []
    for name, a in (("x", x), ("adj", adj), ("v", L0_gnn_input), ("w", L0_gnn_weight)):
        a = np.ascontiguousarray(a)
        arrays[name] = a
        args.append(nc.dram_tensor(name, a.shape, mybir.dt.from_np(a.dtype), kind="ExternalInput").ap())
    y = nc.dram_tensor("y", x.shape, mybir.dt.float32, kind="ExternalOutput").ap()
    gnn_attention(nc, *args, y)
    r = run_bass_kernel_spmd(nc, [arrays], core_ids=[0])
    return r.results[0]["y"]
```

```python
from contextlib import ExitStack

import concourse.bass as bass
from concourse import mybir

ALU = mybir.AluOpType
ACT = mybir.ActivationFunctionType
AX_X = mybir.AxisListType.X
F32 = mybir.dt.float32
F32R = mybir.dt.float32r
I32 = mybir.dt.int32

P = 128
BANK = 512
UNIT = 2 * BANK
TILE = BANK // 2
TEMPERATURE = 0.07
EPS = 1e-5
MASKED = -(2.0 ** 100)
LOWEST = -3.0e38

ADJ_RING = 4
PT_RING = 4
B_TAIL = 2
VT_RING = 3


def gnn_attention(nc, x, adj, inp, weight, out):
    M, D = x.shape
    N = inp.shape[0]
    RB = M // P
    PAIRS = RB // 2
    UNITS = N // UNIT
    STEPS = 2 * N // BANK
    HALF = STEPS // 2
    CH_TILE = TILE // P
    TPU = UNIT // TILE
    T_LAG = STEPS + 4
    PV_LAG = T_LAG + 3
    COPY_AT = PV_LAG - STEPS + 1
    TURN_AT = COPY_AT + 2
    FINISH_AT = TURN_AT + 2
    Q_AT = HALF + 2
    RSTD_STEPS = 6
    assert D == P and PAIRS % 2 == 0 and PAIRS >= 6 and N % UNIT == 0 and N // TILE == STEPS
    assert STEPS % PT_RING == 0 and 2 * UNITS % ADJ_RING == 0 and UNITS % 2 == 0

    with ExitStack() as ctx:
        def sb(name, shape, dt):
            return ctx.enter_context(nc.sbuf_tensor(name, shape, dt))

        def psum(name, shape, dt):
            return ctx.enter_context(nc.psum_tensor(name, shape, dt))

        def sem(name):
            return ctx.enter_context(nc.semaphore(name))

        v_hi = sb("v_hi", [P, N], F32R)
        v_lo = sb("v_lo", [P, N], F32R)
        vt_hi = sb("vt_hi", [P, N], F32R)
        vt_lo = sb("vt_lo", [P, N], F32R)
        probs_a = sb("probs_a", [P, 2, N], F32)
        probs_b = sb("probs_b", [P, N + B_TAIL * UNIT], F32)
        adj_in = sb("adj_in", [P, ADJ_RING, UNIT], I32)
        pt_hi = sb("pt_hi", [P, PT_RING, CH_TILE, 2, P], F32R)
        pt_lo = sb("pt_lo", [P, PT_RING, CH_TILE, 2, P], F32R)
        w_sb = sb("w_sb", [P, D], F32)
        ident = sb("ident", [P, P], F32)
        x_ln = sb("x_ln", [P, 2, D], F32)
        x_res = sb("x_res", [P, 2, D], F32)
        h_norm = sb("h_norm", [P, 2, D], F32)
        h_t = sb("h_t", [P, 2 * P], F32)
        q_full = sb("q_full", [P, 2 * P], F32)
        q_hi = sb("q_hi", [P, 2, 2 * P], F32R)
        q_lo = sb("q_lo", [P, 2, 2 * P], F32R)
        stats = sb("stats", [P, 2, 6], F32)
        moments = sb("moments", [P, 2, 2], F32)
        variance = sb("variance", [P, 2], F32)
        root = sb("root", [P, 2], F32)
        root_check = sb("root_check", [P, 3, 2], F32)
        rstd = sb("rstd", [P, 2], F32)
        minus_half = sb("minus_half", [P, 2], F32)
        unit_max = sb("unit_max", [P, 2, UNITS], F32)
        neg_max = sb("neg_max", [P, 2], F32)
        unit_sum = sb("unit_sum", [P, 2, UNITS], F32)
        row_sum = sb("row_sum", [P, 2], F32)
        inv_sum = sb("inv_sum", [P, 2, 2], F32)
        out_t = sb("out_t", [P, 2 * P], F32)
        out_sb = sb("out_sb", [P, 2, D], F32)

        ps_scores = psum("ps_scores", [P, 2, UNIT], F32)
        ps_pt = psum("ps_pt", [P, 2, CH_TILE, 2, P], F32)
        ps_out = psum("ps_out", [P, 2, 2, 2 * P], F32)

        v_loaded = [sem(f"v_loaded{u}") for u in range(UNITS)]
        w_loaded = sem("w_loaded")
        x_ln_loaded = sem("x_ln_loaded")
        x_res_loaded = sem("x_res_loaded")
        adj_loaded = [sem(f"adj_loaded{s}") for s in range(ADJ_RING)]
        out_stored = sem("out_stored")
        ident_zeroed = sem("ident_zeroed")
        ident_ready = sem("ident_ready")
        vt_ready = sem("vt_ready")
        vt_hi_done = sem("vt_hi_done")
        vt_lo_done = sem("vt_lo_done")
        v_hi_done = sem("v_hi_done")
        v_lo_done = sem("v_lo_done")
        stats_done = sem("stats_done")
        moments_done = sem("moments_done")
        consts_ready = sem("consts_ready")
        rstd_step = sem("rstd_step")
        norm_done = sem("norm_done")
        ht_ready = sem("ht_ready")
        relu_done = sem("relu_done")
        q_ready = sem("q_ready")
        q_scaled = sem("q_scaled")
        q_lo_done = sem("q_lo_done")
        mask_ready = sem("mask_ready")
        scores_ready = sem("scores_ready")
        masked_done = sem("masked_done")
        max_ready = sem("max_ready")
        exp_done = [sem("exp_a_done"), sem("exp_b_done")]
        pt_ready = sem("pt_ready")
        pt_hi_done = sem("pt_hi_done")
        pt_lo_done = sem("pt_lo_done")
        pv_done = sem("pv_done")
        sum_ready = sem("sum_ready")
        inv_ready = sem("inv_ready")
        out_t_copied = sem("out_t_copied")
        out_turned = sem("out_turned")
        out_ready = sem("out_ready")
        waits_taken = {e: sem(f"waits_taken_{e.name}") for e in (mybir.EngineType.DVE, mybir.EngineType.Pool)}

        block = ctx.enter_context(nc.Block())

        def tile_behind(i, par, g, lag):
            t = STEPS + g - lag
            if t >= 0:
                return 2 * i + par - 1, (par + 1) % 2, t
            return 2 * i + par - 2, par, t + STEPS

        def exists(i, j):
            return not isinstance(i, int) or 0 <= j < PAIRS

        def later(i, n, least):
            return not isinstance(i, int) or n >= least

        def run_pairs(eng, pair):
            pair(0, 0)
            pair(0, 1)
            with eng.Fori(1, PAIRS // 2 - 1) as i:
                pair(i, 0)
                pair(i, 1)
            pair(PAIRS // 2 - 1, 0)
            pair(PAIRS // 2 - 1, 1)

        def rows(i, par, shift=0, n=2):
            first = int((par + shift) * 2 * P)
            return bass.ds(i * (4 * P) + first, n * P)

        def probs(b, par, col, n):
            if b == 0:
                return probs_a[:, par, col:col + n]
            if col >= N - B_TAIL * UNIT:
                col += par * B_TAIL * UNIT
            return probs_b[:, col:col + n]

        def hold_sequencer(eng):
            eng.sem_inc(waits_taken[eng.engine], 1)

        v_stage = probs_a[:, 1, :]

        def ps_vt(h):
            if h % VT_RING < 2:
                return ps_pt[:, h % VT_RING].rearrange("p c b m -> p (c b m)")
            return ps_out[:, 0].rearrange("p n m -> p (n m)")

        @block.sync
        def _(sp):
            def load_x_ln(i, par, shift):
                sp.dma_start(x_ln[:], x[rows(i, par, shift), :].rearrange("(b p) d -> p b d", p=P)
                             ).then_inc(x_ln_loaded, 16)

            def load_v(u):
                cu = UNIT // P
                sp.dma_start(v_stage[:, u * UNIT:(u + 1) * UNIT].rearrange("p (c d) -> p c d", d=D),
                             inp.rearrange("(c p) d -> p c d", p=P)[:, u * cu:(u + 1) * cu, :]
                             ).then_inc(v_loaded[u], 16)

            load_x_ln(0, 0, 0)
            sp.dma_start(w_sb[:], weight).then_inc(w_loaded, 16)
            load_v(0)

            def pair(i, par):
                j = 2 * i + par
                for n in range(2 * UNITS):
                    b, u = n // UNITS, n % UNITS
                    slot = n % ADJ_RING
                    if later(i, 2 * UNITS * j + n, ADJ_RING):
                        sp.wait_ge(masked_done, 2 * UNITS * j + n - ADJ_RING + 1)
                    sp.dma_start(adj_in[:, slot, :],
                                 adj[rows(i, par, b / 2, 1), u * UNIT:(u + 1) * UNIT]).then_inc(adj_loaded[slot], 16)
                    if isinstance(i, int) and j == 0 and n < ADJ_RING:
                        for v in range(n + 1, UNITS if n == ADJ_RING - 1 else n + 2):
                            load_v(v)
                    if n == 2 and exists(i, j + 1):
                        sp.wait_ge(norm_done, j + 1)
                        load_x_ln(i, par, 1)
                    if n == 2 * UNITS - 2:
                        store_and_reload(i, par)

            def store_and_reload(i, par):
                j = 2 * i + par
                if exists(i, j - 2):
                    sp.wait_ge(out_ready, j - 1)
                    sp.dma_start(out[rows(i, par, -2), :].rearrange("(b p) d -> p b d", p=P), out_sb[:]
                                 ).then_inc(out_stored, 16)
                if exists(i, j - 1):
                    sp.dma_start(x_res[:], x[rows(i, par, -1), :].rearrange("(b p) d -> p b d", p=P)
                                 ).then_inc(x_res_loaded, 16)

            run_pairs(sp, pair)
            store_and_reload(PAIRS // 2, 0)
            store_and_reload(PAIRS // 2, 1)
            sp.wait_ge(out_stored, 16 * PAIRS)

        @block.gpsimd
        def _(pool):
            nc.gpsimd.memset(ident[:], 0.0).then_inc(ident_zeroed, 1)
            pool.wait_ge(ident_zeroed, 1)
            nc.gpsimd.affine_select(out=ident[:], in_=ident[:], compare_op=ALU.not_equal, fill=1.0,
                                    base=0, pattern=[[-1, P]], channel_multiplier=1).then_inc(ident_ready, 1)

            nc.gpsimd.memset(minus_half[:], -0.5).then_inc(consts_ready, 1)
            pool.wait_ge(consts_ready, 1)

            def deviation(j):
                taken = [0]

                def step(ins):
                    taken[0] += 1
                    ins.then_inc(rstd_step, 1)
                    pool.wait_ge(rstd_step, RSTD_STEPS * j + taken[0])
                    hold_sequencer(pool)

                pool.wait_ge(moments_done, j + 1)
                hold_sequencer(pool)
                step(nc.gpsimd.tensor_scalar(variance[:], moments[:, :, 1], EPS, None, ALU.add))
                step(nc.gpsimd.tensor_tensor(root[:], variance[:], minus_half[:], ALU.pow))
                step(nc.gpsimd.tensor_tensor(root_check[:, 0, :], root[:], root[:], ALU.mult))
                step(nc.gpsimd.tensor_tensor(root_check[:, 1, :], root_check[:, 0, :], variance[:], ALU.mult))
                step(nc.gpsimd.tensor_scalar(root_check[:, 2, :], root_check[:, 1, :], -0.5, 1.5,
                                             ALU.mult, ALU.add))
                step(nc.gpsimd.tensor_tensor(rstd[:], root[:], root_check[:, 2, :], ALU.mult))
                assert taken[0] == RSTD_STEPS

            def normalise(j):
                deviation(j)
                if later(j, j, 1):
                    pool.wait_ge(ht_ready, j)
                hold_sequencer(pool)
                for b in range(2):
                    last = nc.gpsimd.tensor_scalar(h_norm[:, b, :], x_ln[:, b, :], moments[:, b, 0:1],
                                                   rstd[:, b:b + 1], ALU.subtract, ALU.mult)
                last.then_inc(norm_done, 1)

            def split_q(j, par):
                pool.wait_ge(q_scaled, 2 * j + 2)
                nc.gpsimd.tensor_tensor(q_lo[:, par, :], q_full[:], q_hi[:, par, :].bitcast(F32),
                                        ALU.subtract).then_inc(q_lo_done, 1)

            deviation(0)
            split_q(0, 0)

            def split_v(u):
                cols = slice(u * UNIT, (u + 1) * UNIT)
                pool.wait_ge(v_hi_done, u + 1)
                nc.gpsimd.tensor_tensor(v_lo[:, cols], v_stage[:, cols], v_hi[:, cols].bitcast(F32),
                                        ALU.subtract).then_inc(v_lo_done, 1)

            def pair(i, par):
                j = 2 * i + par
                if exists(i, j + 1):
                    if isinstance(i, int) and j == 0:
                        split_v(0)
                    normalise(j + 1)
                    if isinstance(i, int) and j == 0:
                        for u in range(1, UNITS):
                            split_v(u)
                    split_q(j + 1, (par + 1) % 2)

            run_pairs(pool, pair)

        @block.tensor
        def _(pe):
            def transpose_h(j, par):
                pe.wait_ge(norm_done, j + 1)
                if later(j, j, 3):
                    pe.wait_ge(out_ready, j - 2)
                for b in range(2):
                    last = nc.tensor.transpose(ps_out[:, (par + 1) % 2, 0, b * P:(b + 1) * P], h_norm[:, b, :],
                                               ident[:])
                last.then_inc(ht_ready, 1)

            def project_q(j, par):
                pe.wait_ge(relu_done, j + 1)
                nc.tensor.matmul(ps_out[:, (par + 1) % 2, 1, :], w_sb[:], h_t[:], start=True, stop=True
                                 ).then_inc(q_ready, 1)

            def scores(i, par, g):
                j, b, k = 2 * i + par, g // HALF, g % HALF
                unit = 2 * UNITS * j + g // 2
                if g == 0:
                    pe.wait_ge(q_lo_done, j + 1)
                if g % 2 == 0 and later(i, unit, 2):
                    pe.wait_ge(masked_done, unit - 1)
                dst = ps_scores[:, (g // 2) % 2, (g % 2) * BANK:(g % 2 + 1) * BANK]
                cols = slice(k * BANK, (k + 1) * BANK)
                q = slice(b * P, (b + 1) * P)
                nc.tensor.matmul(dst, q_hi[:, par, q], vt_hi[:, cols], start=True, stop=False)
                nc.tensor.matmul(dst, q_hi[:, par, q], vt_lo[:, cols], start=False, stop=False)
                last = nc.tensor.matmul(dst, q_lo[:, par, q], vt_hi[:, cols], start=False, stop=True)
                if g % 2 == 1:
                    last.then_inc(scores_ready, 1)

            def transpose_probs(j, par, t):
                if t % TPU == 0:
                    pe.wait_ge(exp_done[0], UNITS * j + t // TPU + 1)
                    pe.wait_ge(exp_done[1], UNITS * j + t // TPU + 1)
                if later(j, STEPS * j + t, 2):
                    pe.wait_ge(pt_lo_done, STEPS * j + t - 1)
                for c in range(CH_TILE):
                    for b in range(2):
                        last = nc.tensor.transpose(ps_pt[:, t % 2, c, b, :], probs(b, par, t * TILE + c * P, P),
                                                   ident[:])
                last.then_inc(pt_ready, 1)

            def times_v(j, par, t):
                if t == 0 and later(j, j, 2):
                    pe.wait_ge(out_ready, j - 1)
                if isinstance(j, int) and j == 0 and t % TPU == 0:
                    pe.wait_ge(v_lo_done, t // TPU + 1)
                pe.wait_ge(pt_lo_done, STEPS * j + t + 1)
                acc = ps_out[:, par, 0, :]
                for c in range(CH_TILE):
                    ch = t * CH_TILE + c
                    v = slice(ch * P, (ch + 1) * P)
                    hi = pt_hi[:, t % PT_RING, c, :, :].rearrange("p b m -> p (b m)")
                    lo = pt_lo[:, t % PT_RING, c, :, :].rearrange("p b m -> p (b m)")
                    nc.tensor.matmul(acc, v_hi[:, v], hi, start=(ch == 0), stop=False)
                    nc.tensor.matmul(acc, v_lo[:, v], hi, start=False, stop=False)
                    last = nc.tensor.matmul(acc, v_hi[:, v], lo, start=False, stop=(ch == N // P - 1))
                last.then_inc(pv_done, 1)

            def turn_out(j, par):
                pe.wait_ge(out_t_copied, j + 1)
                for b in range(2):
                    last = nc.tensor.transpose(ps_out[:, par, 1, b * P:(b + 1) * P], out_t[:, b * P:(b + 1) * P],
                                               ident[:])
                last.then_inc(out_turned, 1)

            def transpose_v(h):
                if h % 2 == 0:
                    pe.wait_ge(v_loaded[h // 2], 16)
                if h >= VT_RING:
                    pe.wait_ge(vt_lo_done, h - VT_RING + 1)
                for c in range(BANK // P):
                    last = nc.tensor.transpose(ps_vt(h)[:, c * P:(c + 1) * P],
                                               v_stage[:, h * BANK + c * P:h * BANK + (c + 1) * P], ident[:])
                last.then_inc(vt_ready, 1)

            def pair(i, par):
                j = 2 * i + par
                for g in range(STEPS):
                    if isinstance(i, int) and j == 0 and g < HALF:
                        pe.wait_ge(vt_lo_done, g + 1)
                    if exists(i, j):
                        scores(i, par, g)
                    if isinstance(i, int) and j == 0 and g + VT_RING < HALF:
                        transpose_v(g + VT_RING)
                    tj, tpar, t = tile_behind(i, par, g, T_LAG)
                    if exists(i, tj):
                        transpose_probs(tj, tpar, t)
                    tj, tpar, t = tile_behind(i, par, g, PV_LAG)
                    if exists(i, tj):
                        times_v(tj, tpar, t)
                    if g == TURN_AT and exists(i, j - 2):
                        turn_out(j - 2, par)
                    if g == Q_AT and exists(i, j + 1):
                        transpose_h(j + 1, (par + 1) % 2)
                    if g == Q_AT + 2 and exists(i, j + 1):
                        project_q(j + 1, (par + 1) % 2)

            pe.wait_ge(ident_ready, 1)
            transpose_v(0)
            transpose_v(1)
            transpose_h(0, 0)
            transpose_v(2)
            pe.wait_ge(w_loaded, 16)
            project_q(0, 0)
            pair(0, 0)
            pair(0, 1)
            with pe.Fori(1, PAIRS // 2 - 1) as i:
                pair(i, 0)
                pair(i, 1)
            pair(PAIRS // 2 - 1, 0)
            pair(PAIRS // 2 - 1, 1)
            pair(PAIRS // 2, 0)
            pair(PAIRS // 2, 1)

        @block.scalar
        def _(act):
            def relu_h(j, par):
                act.wait_ge(ht_ready, j + 1)
                if later(j, j, 1):
                    act.wait_ge(q_ready, j)
                nc.scalar.activation(h_t[:], ps_out[:, (par + 1) % 2, 0, :], ACT.Relu).then_inc(relu_done, 1)

            def scale_q(j, par):
                q = ps_out[:, (par + 1) % 2, 1, :]
                act.wait_ge(q_ready, j + 1)
                if later(j, j, 1):
                    act.wait_ge(q_lo_done, j)
                nc.scalar.mul(q_full[:], q, 1.0 / TEMPERATURE).then_inc(q_scaled, 1)
                if later(j, j, 2):
                    act.wait_ge(scores_ready, 2 * UNITS * (j - 1))
                nc.scalar.mul(q_hi[:, par, :], q, 1.0 / TEMPERATURE).then_inc(q_scaled, 1)

            def split_hi(j, t):
                act.wait_ge(pt_ready, STEPS * j + t + 1)
                if later(j, STEPS * j + t, PT_RING):
                    act.wait_ge(pv_done, STEPS * j + t - PT_RING + 1)
                nc.scalar.copy(pt_hi[:, t % PT_RING], ps_pt[:, t % 2]).then_inc(pt_hi_done, 1)

            def exponent(j, par, b, u):
                if u == 0:
                    act.wait_ge(max_ready, 2 * j + b + 1)
                    if later(j, j, 1):
                        act.wait_ge(sum_ready, 2 * j + b - 1)
                piece = probs(b, par, u * UNIT, UNIT)
                nc.scalar.activation(piece, piece, ACT.Exp, bias=neg_max[:, b:b + 1], scale=1.0,
                                     accum_out=unit_sum[:, b, u:u + 1]).then_inc(exp_done[b], 1)

            def copy_out_t(j, par):
                act.wait_ge(pv_done, STEPS * (j + 1))
                if later(j, j, 1):
                    act.wait_ge(out_turned, j)
                nc.scalar.copy(out_t[:], ps_out[:, par, 0, :]).then_inc(out_t_copied, 1)

            def pair(i, par):
                j = 2 * i + par
                for g in range(STEPS):
                    tj, _, t = tile_behind(i, par, g, T_LAG)
                    if exists(i, tj):
                        split_hi(tj, t)
                    if g % TPU == 0 and exists(i, j - 1):
                        exponent(j - 1, (par + 1) % 2, 1, g // TPU)
                    if g % TPU == 2:
                        u = (g - HALF) // TPU
                        if u >= 0 and exists(i, j):
                            exponent(j, par, 0, u)
                        if u < 0 and exists(i, j - 1):
                            exponent(j - 1, (par + 1) % 2, 0, u + UNITS)
                    if g == COPY_AT and exists(i, j - 2):
                        copy_out_t(j - 2, par)
                    if g == Q_AT + 1 and exists(i, j + 1):
                        relu_h(j + 1, (par + 1) % 2)
                    if g == Q_AT + 3 and exists(i, j + 1):
                        scale_q(j + 1, (par + 1) % 2)

            def split_vt(h):
                cols = slice(h * BANK, (h + 1) * BANK)
                act.wait_ge(vt_ready, h + 1)
                nc.scalar.copy(vt_hi[:, cols], ps_vt(h)).then_inc(vt_hi_done, 1)

            def split_v(u):
                cols = slice(u * UNIT, (u + 1) * UNIT)
                act.wait_ge(v_loaded[u], 16)
                nc.scalar.copy(v_hi[:, cols], v_stage[:, cols]).then_inc(v_hi_done, 1)

            split_vt(0)
            split_vt(1)
            relu_h(0, 0)
            split_vt(2)
            scale_q(0, 0)
            for h in range(VT_RING, HALF):
                split_vt(h)
                if h % 2 == 0:
                    split_v(h // 2 - 2)
            for u in range(HALF // 2 - 2, UNITS):
                split_v(u)
            run_pairs(act, pair)
            pair(PAIRS // 2, 0)
            pair(PAIRS // 2, 1)

        @block.vector
        def _(dve):
            def row_stats(j):
                dve.wait_ge(x_ln_loaded, 16 * (j + 1))
                for b in range(2):
                    last = nc.vector.bn_stats(stats[:, b, :], x_ln[:, b, :])
                last.then_inc(stats_done, 1)

            def row_moments(j):
                dve.wait_ge(stats_done, j + 1)
                if later(j, j, 1):
                    dve.wait_ge(norm_done, j)
                hold_sequencer(dve)
                for b in range(2):
                    last = nc.vector.bn_aggr(moments[:, b, :], stats[:, b, :])
                last.then_inc(moments_done, 1)

            def normalise_first():
                dve.wait_ge(rstd_step, RSTD_STEPS)
                for b in range(2):
                    last = nc.vector.tensor_scalar(h_norm[:, b, :], x_ln[:, b, :], moments[:, b, 0:1],
                                                   rstd[:, b:b + 1], ALU.subtract, ALU.mult)
                last.then_inc(norm_done, 1)

            def split_vt(h):
                cols = slice(h * BANK, (h + 1) * BANK)
                dve.wait_ge(vt_hi_done, h + 1)
                nc.vector.tensor_tensor(vt_lo[:, cols], ps_vt(h), vt_hi[:, cols].bitcast(F32),
                                        ALU.subtract).then_inc(vt_lo_done, 1)

            def make_mask(i, par, n):
                slot, per_pair = n % ADJ_RING, 2 * UNITS // ADJ_RING
                dve.wait_ge(adj_loaded[slot], 16 * (i * (2 * per_pair) + par * per_pair + n // ADJ_RING + 1))
                nc.vector.tensor_scalar(adj_in[:, slot, :].bitcast(F32), adj_in[:, slot, :], 0.0, MASKED,
                                        ALU.is_le, ALU.mult).then_inc(mask_ready, 1)

            def add_mask(i, par, n):
                j, b, u = 2 * i + par, n // UNITS, n % UNITS
                unit = 2 * UNITS * j + n
                dve.wait_ge(scores_ready, unit + 1)
                dve.wait_ge(mask_ready, unit + 1)
                back = 1 if b == 1 and u < UNITS - B_TAIL else 2
                if later(i, j, back):
                    dve.wait_ge(pt_ready, STEPS * (j - back) + TPU * (u + 1))
                if isinstance(i, int) and j == 1 and b == 0:
                    dve.wait_ge(v_lo_done, u + 1)
                hold_sequencer(dve)
                nc.vector.tensor_tensor_reduce(
                    out=probs(b, par, u * UNIT, UNIT), in0=ps_scores[:, n % 2, :],
                    in1=adj_in[:, n % ADJ_RING, :].bitcast(F32), scale=1.0, scalar=LOWEST,
                    op0=ALU.add, op1=ALU.max, accum_out=unit_max[:, b, u:u + 1]).then_inc(masked_done, 1)

            def row_max(i, par, b):
                j = 2 * i + par
                dve.wait_ge(masked_done, UNITS * (2 * j + b + 1))
                if later(i, j, 1):
                    dve.wait_ge(exp_done[b], UNITS * j)
                nc.vector.tensor_reduce(neg_max[:, b:b + 1], unit_max[:, b, :], AX_X, ALU.max,
                                        negate=True).then_inc(max_ready, 1)

            def split_lo(j, t):
                dve.wait_ge(pt_hi_done, STEPS * j + t + 1)
                nc.vector.tensor_tensor(pt_lo[:, t % PT_RING], ps_pt[:, t % 2],
                                        pt_hi[:, t % PT_RING].bitcast(F32), ALU.subtract).then_inc(pt_lo_done, 1)

            def invert_sum(j, par, b):
                dve.wait_ge(exp_done[b], UNITS * (j + 1))
                nc.vector.reduce_sum(row_sum[:, b:b + 1], unit_sum[:, b, :], AX_X).then_inc(sum_ready, 1)
                dve.wait_ge(sum_ready, 2 * j + b + 1)
                nc.vector.reciprocal(inv_sum[:, par, b:b + 1], row_sum[:, b:b + 1]).then_inc(inv_ready, 1)

            def finish(j, par):
                dve.wait_ge(out_turned, j + 1)
                dve.wait_ge(inv_ready, 2 * j + 2)
                dve.wait_ge(x_res_loaded, 16 * (j + 1))
                if later(j, j, 1):
                    dve.wait_ge(out_stored, 16 * j)
                for b in range(2):
                    last = nc.vector.scalar_tensor_tensor(
                        out=out_sb[:, b, :], in0=ps_out[:, par, 1, b * P:(b + 1) * P],
                        scalar=inv_sum[:, par, b:b + 1], in1=x_res[:, b, :], op0=ALU.mult, op1=ALU.add)
                last.then_inc(out_ready, 1)

            def pair(i, par):
                j = 2 * i + par
                for g in range(STEPS):
                    if g % 2 == 0 and exists(i, j):
                        make_mask(i, par, g // 2)
                    if g == 2 and exists(i, j + 1):
                        row_stats(j + 1)
                    if g == 3 and exists(i, j + 1):
                        row_moments(j + 1)
                    tj, _, t = tile_behind(i, par, g, T_LAG)
                    if exists(i, tj):
                        split_lo(tj, t)
                    if g % 2 == 1 and exists(i, j):
                        add_mask(i, par, g // 2)
                        if g % HALF == HALF - 1:
                            row_max(i, par, g // HALF)
                    if isinstance(i, int) and j == 0 and g + VT_RING < HALF:
                        split_vt(g + VT_RING)
                    if g == FINISH_AT and exists(i, j - 2):
                        finish(j - 2, par)
                    if g == HALF and exists(i, j - 1):
                        invert_sum(j - 1, (par + 1) % 2, 0)
                    if g == STEPS - 2 and exists(i, j - 1):
                        invert_sum(j - 1, (par + 1) % 2, 1)

            row_stats(0)
            row_moments(0)
            normalise_first()
            for h in range(VT_RING):
                split_vt(h)
            run_pairs(dve, pair)
            pair(PAIRS // 2, 0)
            pair(PAIRS // 2, 1)


def kernel(x, adj, L0_gnn_input, L0_gnn_weight):
    import numpy as np
    import concourse.bacc as bacc
    from concourse.bass_utils import run_bass_kernel_spmd

    nc = bacc.Bacc("TRN2", target_bir_lowering=False, num_devices=1, dynamic_dma_scratch_size=1024)
    arrays, args = {}, []
    for name, a in (("x", x), ("adj", adj), ("v", L0_gnn_input), ("w", L0_gnn_weight)):
        a = np.ascontiguousarray(a)
        arrays[name] = a
        args.append(nc.dram_tensor(name, a.shape, mybir.dt.from_np(a.dtype), kind="ExternalInput").ap())
    y = nc.dram_tensor("y", x.shape, mybir.dt.float32, kind="ExternalOutput").ap()
    gnn_attention(nc, *args, y)
    r = run_bass_kernel_spmd(nc, [arrays], core_ids=[0])
    return r.results[0]["y"]
```
